# Optimizing a Trainium2 kernel written in Bass

```python
import numpy as np
import jax
import jax.numpy as jnp

def _softmax(x, axis=-1):
    return jax.nn.softmax(x, axis=axis)

def _gelu(x):
    return jax.nn.gelu(x, approximate=True)

def _silu(x):
    return jax.nn.silu(x)

def _sigmoid(x):
    return jax.nn.sigmoid(x)

def _layernorm(x, axis=-1, eps=1e-05):
    m = jnp.mean(x, axis=axis, keepdims=True)
    v = jnp.var(x, axis=axis, keepdims=True)
    return (x - m) / jnp.sqrt(v + eps)

def _scatter_add(tgt, idx, src, axis=0):
    return tgt.at[idx].add(src)

def _segment_sum(src, seg, n):
    return jax.ops.segment_sum(src, seg, n)
kernel_name = 'mk_adaln_ffn_d1_seqx_r8_a8d7c8'

def setup_inputs(seed: int=0):
    np.random.seed(seed)
    _w = jnp.asarray

    def _rec_inputs():
        import jax
        import jax.numpy as jnp
        _rk = jax.random.key(seed)
        x = -0.000125 + 0.9999 * jax.random.normal(jax.random.fold_in(_rk, 1), (8, 128, 512), jnp.float32)
        _lenS = 128 - jax.random.randint(jax.random.fold_in(_rk, 7), (8,), 0, max(1, 128 // 4) + 1, jnp.int32)
        _lenS2 = 128 - jax.random.randint(jax.random.fold_in(_rk, 8), (8,), 0, max(1, 128 // 4) + 1, jnp.int32)
        itok_B_0_7 = jax.random.randint(jax.random.fold_in(_rk, 11), (8,), 0, 8, jnp.int32)
        return (x, itok_B_0_7)
    x, itok_B_0_7 = _rec_inputs()

    def _L0_cond_setup():
        import jax, jax.numpy as jnp
        import numpy as np
        TOP_K = 2
        LANG_BIAS = 5.0
        SCALING = 32.0 / 16.0
        LANGUAGE_PAD_ID = -1
        key = jax.random.key(seed)
        ks = jax.random.split(key, 6)
        B, T, D, O, E, R = (4, 256, 512, 512, 8, 16)
        x = jax.random.normal(ks[0], (B, T, D), dtype=jnp.float32)
        language_ids = jax.random.randint(ks[1], (B,), 0, E).astype(jnp.int64)
        W = jax.random.normal(ks[2], (O, D), dtype=jnp.float32) * (1.0 / np.sqrt(D))
        Wr = jax.random.normal(ks[3], (E, D), dtype=jnp.float32) * (1.0 / np.sqrt(D))
        A = jax.random.normal(ks[4], (E, R, D), dtype=jnp.float32) * (1.0 / np.sqrt(D))
        Bm = jax.random.normal(ks[5], (O, R), dtype=jnp.float32) * 0.0
        Bm = jnp.broadcast_to(Bm, (E, O, R)) + jax.random.normal(ks[5], (E, O, R), dtype=jnp.float32) * 0.02
        return {'x': x, 'language_ids': language_ids, 'W': W, 'Wr': Wr, 'A': A, 'B': Bm}
    _L0_cond_all = _L0_cond_setup()
    _L0_cond_in = {k: v for k, v in _L0_cond_all.items() if k in ('W', 'Wr', 'A', 'B')}
    del _L0_cond_all

    def _L0_ffn_setup():
        import jax, jax.numpy as jnp
        import numpy as np
        NUM_EXPERTS = 8
        TOP_K = 2
        RANK = 16
        LORA_ALPHA = 32
        SCALING = LORA_ALPHA / RANK
        key = jax.random.key(seed)
        ks = jax.random.split(key, 6)
        B, S, D_IN, D_OUT = (4, 256, 512, 512)
        x = jax.random.normal(ks[0], (B, S, D_IN), dtype=jnp.float32)
        W_base = jax.random.normal(ks[1], (D_OUT, D_IN), dtype=jnp.float32) * 0.02
        b_base = jax.random.normal(ks[2], (D_OUT,), dtype=jnp.float32) * 0.02
        W_router = jax.random.normal(ks[3], (NUM_EXPERTS, D_IN), dtype=jnp.float32) * 0.02
        A = jax.random.normal(ks[4], (NUM_EXPERTS, RANK, D_IN), dtype=jnp.float32) * 0.02
        Bm = jax.random.normal(ks[5], (D_OUT, RANK), dtype=jnp.float32) * 0.02
        Bm = jnp.broadcast_to(Bm, (NUM_EXPERTS, D_OUT, RANK)) * jnp.arange(1, NUM_EXPERTS + 1, dtype=jnp.float32)[:, None, None] * 0.2
        return {'x': x, 'W_base': W_base, 'b_base': b_base, 'W_router': W_router, 'A': A, 'B': Bm}
    _L0_ffn_all = _L0_ffn_setup()
    _L0_ffn_in = {k: v for k, v in _L0_ffn_all.items() if k in ('W_base', 'b_base', 'W_router', 'A', 'B')}
    del _L0_ffn_all
    return {'x': x, 'itok_B_0_7': itok_B_0_7, 'L0_cond_W': _L0_cond_in['W'], 'L0_cond_Wr': _L0_cond_in['Wr'], 'L0_cond_A': _L0_cond_in['A'], 'L0_cond_B': _L0_cond_in['B'], 'L0_ffn_W_base': _L0_ffn_in['W_base'], 'L0_ffn_b_base': _L0_ffn_in['b_base'], 'L0_ffn_W_router': _L0_ffn_in['W_router'], 'L0_ffn_A': _L0_ffn_in['A'], 'L0_ffn_B': _L0_ffn_in['B']}

def reference(x, itok_B_0_7, L0_cond_W, L0_cond_Wr, L0_cond_A, L0_cond_B, L0_ffn_W_base, L0_ffn_b_base, L0_ffn_W_router, L0_ffn_A, L0_ffn_B):
    import jax
    import jax.numpy as jnp

    def _L0_cond_ref(x, language_ids, W, Wr, A, B):
        import jax, jax.numpy as jnp
        import numpy as np
        TOP_K = 2
        LANG_BIAS = 5.0
        SCALING = 32.0 / 16.0
        LANGUAGE_PAD_ID = -1
        base = jnp.einsum('btd,od->bto', x, W)
        E = Wr.shape[0]
        logits = jnp.einsum('btd,ed->bte', x.astype(jnp.float32), Wr.astype(jnp.float32))
        expert_targets = language_ids
        valid = expert_targets >= 0
        tgt = jnp.where(valid, expert_targets, 0)
        bias = jax.nn.one_hot(tgt, E, dtype=logits.dtype) * LANG_BIAS
        bias = jnp.where(valid[:, None], bias, 0.0)
        logits = logits + bias[:, None, :]
        topw, topi = jax.lax.top_k(logits, TOP_K)
        weights = jax.nn.softmax(topw, axis=-1)
        gates = jnp.sum(jax.nn.one_hot(topi, E, dtype=weights.dtype) * weights[..., None], axis=-2)
        gates = gates.astype(x.dtype)
        h = jnp.einsum('btd,erd->bter', x, A)
        lora_out = jnp.einsum('bter,bte,eor->bto', h, gates, B)
        return base + SCALING * lora_out

    def _L0_ffn_ref(x, W_base, b_base, W_router, A, B):
        import jax, jax.numpy as jnp
        import numpy as np
        NUM_EXPERTS = 8
        TOP_K = 2
        RANK = 16
        LORA_ALPHA = 32
        SCALING = LORA_ALPHA / RANK
        bs, seq, d_in = x.shape
        T = bs * seq
        xf = x.reshape(T, d_in)
        base = xf @ W_base.T + b_base
        logits = xf @ W_router.T
        rw, sel = jax.lax.top_k(logits, TOP_K)
        rw = jax.nn.softmax(rw, axis=-1)
        onehot = jax.nn.one_hot(sel, NUM_EXPERTS, dtype=rw.dtype)
        w = jnp.einsum('tk,tke->te', rw, onehot)
        h = jnp.einsum('td,erd->ter', xf, A)
        lora = jnp.einsum('ter,te,eor->to', h, w, B) * SCALING
        return (base + lora).reshape(bs, seq, -1)
    x = x + _L0_ffn_ref(_L0_cond_ref(x, itok_B_0_7, L0_cond_W, L0_cond_Wr, L0_cond_A, L0_cond_B), L0_ffn_W_base, L0_ffn_b_base, L0_ffn_W_router, L0_ffn_A, L0_ffn_B)
    return x

_drawn_inputs = setup_inputs


def setup_inputs(seed=0):
    import zlib

    import numpy as np

    out = dict(_drawn_inputs(seed))
    spreads = {}
    factors = {'L0_cond_Wr': 7.535, 'L0_ffn_b_base': 3.134}
    for name, (base, spread) in spreads.items():
        noise = np.random.default_rng([zlib.crc32(name.encode()), seed]).standard_normal(out[name].shape)
        drawn = base * np.exp(spread * noise) if base else spread * noise
        out[name] = jnp.asarray(drawn.astype(out[name].dtype))
    for name, factor in factors.items():
        out[name] = (out[name] * factor).astype(out[name].dtype)
    return out
```

```python
import concourse.bass as bass
from concourse import mybir
from contextlib import ExitStack

P = 128
D = 512
KC = D // P
E = 8
R = 16
ER = E * R
NB = 8
TOKENS = NB * P
HALVES = 2
HT = TOKENS // HALVES
TILES = HT // P
SM = ER + E
CW = 2 * SM + D
M2W = SM + D
RA = M2W // 2
RB = M2W - RA
S1W = D + ER
NS = S1W // P
LANG_BIAS = 5.0
WARMUPS = 9


def adaln_ffn(nc: bass.Bass, s1_d, xt_d, m1_d, m2b_d, b2_d, bias_d, ids_d, out_d):
    f32, f32r = mybir.dt.float32, mybir.dt.float32r
    i32, u32 = mybir.dt.int32, mybir.dt.uint32
    ALU = mybir.AluOpType
    ACT = mybir.ActivationFunctionType

    with ExitStack() as ctx:
        def sb(name, shape, dt):
            return ctx.enter_context(nc.sbuf_tensor(name, shape, dt))

        def sem(name):
            return ctx.enter_context(nc.semaphore(name))

        s1 = sb("s1", [P, KC, S1W + RA], f32)
        m2b = sb("m2b", [P, KC, RB], f32)
        m1 = sb("m1", [P, KC, SM], f32)
        b2 = sb("b2", [P, D], f32)
        xt = sb("xt", [P, HALVES, KC, HT], f32)
        bias = sb("bias", [P, KC], f32)
        ids = sb("ids", [P, NB], i32)
        s1_h, s1_l = sb("s1_h", [P, KC, S1W + RA], f32r), sb("s1_l", [P, KC, S1W + RA], f32r)
        m2b_h, m2b_l = sb("m2b_h", [P, KC, RB], f32r), sb("m2b_l", [P, KC, RB], f32r)
        b2_h, b2_l = sb("b2_h", [P, D], f32r), sb("b2_l", [P, D], f32r)
        xt_h, xt_l = sb("xt_h", [P, HALVES, KC, HT], f32r), sb("xt_l", [P, HALVES, KC, HT], f32r)
        cw_h, cw_l = sb("cw_h", [P, NS, CW], f32r), sb("cw_l", [P, NS, CW], f32r)
        gt_h, gt_l = sb("gt_h", [P, 2, HALVES, HT], f32r), sb("gt_l", [P, 2, HALVES, HT], f32r)
        ident = sb("ident", [P, P], f32)
        warm = sb("warm", [P, HT], f32r)
        iota_i = sb("iota_i", [P, E], i32)
        iota = sb("iota", [P, E], f32)
        lang = sb("lang", [P, NB, E], f32)
        logit = sb("logit", [P, TILES, E], f32)
        top = sb("top", [P, TILES, E], f32)
        place = sb("place", [P, TILES, E], u32)
        diff = sb("diff", [P, TILES], f32)
        expd = sb("expd", [P, TILES], f32)
        den = sb("den", [P, TILES], f32)
        pair = sb("pair", [P, TILES, 2], f32)
        hot = sb("hot", [P, TILES, 2, E], f32)
        hotw = sb("hotw", [P, TILES, 2, E], f32)
        gate = sb("gate", [P, TILES, E], f32)
        gated = sb("gated", [P, TILES, ER], f32)
        result = sb("result", [P, KC, HALVES, HT], f32)

        ps = ctx.enter_context(nc.psum_tensor("ps", [P, 8, 512], f32))
        BANK_B = (5, 6, 7, 0, 1)
        BANK_SMALL = 2
        BANK_Z = (6, 7, 0, 1)
        BANK_T = (BANK_Z[3], BANK_SMALL)
        small = ps[:, BANK_SMALL:BANK_SMALL + TILES, :]

        in_s1 = [sem(f"in_s1_{k}") for k in range(KC)]
        in_m2b, in_m1, in_b2 = sem("in_m2b"), sem("in_m1"), sem("in_b2")
        in_bias, in_ids = sem("in_bias"), sem("in_ids")
        in_x = [sem(f"in_x_{h}") for h in range(HALVES)]
        warm_set = sem("warm_set")
        ident_set = sem("ident_set")
        iota_set = sem("iota_set")
        s1_hi, s1_lo = sem("s1_hi"), sem("s1_lo")
        m2b_hi, m2b_lo = sem("m2b_hi"), sem("m2b_lo")
        m1_hi, m1_lo = sem("m1_hi"), sem("m1_lo")
        b2_hi, b2_lo = sem("b2_hi"), sem("b2_lo")
        x_hi, x_lo = sem("x_hi"), sem("x_lo")
        a_done, b_done = sem("a_done"), sem("b_done")
        a_hi, a_lo = sem("a_hi"), sem("a_lo")
        b_hi, b_lo = sem("b_hi"), sem("b_lo")
        small1_done = sem("small1_done")
        small2_done = sem("small2_done")
        exp_in, exp_out = sem("exp_in"), sem("exp_out")
        gated_done = sem("gated_done")
        t_done = sem("t_done")
        t_hi, t_lo = sem("t_hi"), sem("t_lo")
        z_done = sem("z_done")
        z_out = sem("z_out")
        stored = sem("stored")
        dve_step = sem("dve_step")

        block = ctx.enter_context(nc.Block())

        @block.sync
        def _(sp):
            for k in range(KC):
                sp.dma_start(s1[:, k, :], s1_d[k]).then_inc(in_s1[k], 16)
            sp.dma_start(m2b[:], m2b_d).then_inc(in_m2b, 16)
            sp.dma_start(m1[:], m1_d).then_inc(in_m1, 16)
            for h in range(HALVES):
                sp.dma_start(xt[:, h], xt_d[h]).then_inc(in_x[h], 16)
                if h == 0:
                    sp.dma_start(ids[:], ids_d).then_inc(in_ids, 16)
            sp.dma_start(b2[:], b2_d).then_inc(in_b2, 16)
            sp.dma_start(bias[:], bias_d).then_inc(in_bias, 16)
            for n in range(HALVES * KC):
                h, j = n // KC, n % KC
                sp.wait_ge(z_out, n + 1)
                sp.dma_start(out_d[h, j], result[:, j, h, :]).then_inc(stored, 16)
            sp.wait_ge(stored, 16 * HALVES * KC)

        @block.gpsimd
        def _(pool):
            nc.gpsimd.memset(ident[:], 0.0).then_inc(ident_set, 1)
            nc.gpsimd.iota(iota_i[:], [[1, E]], base=0, channel_multiplier=0).then_inc(iota_set, 1)
            pool.wait_ge(ident_set, 1)
            nc.gpsimd.affine_select(out=ident[:], in_=ident[:], compare_op=ALU.not_equal, fill=1.0, base=0,
                                    pattern=[[-1, P]], channel_multiplier=1).then_inc(ident_set, 1)

        @block.scalar
        def _(act):
            def hi_x(h, k):
                if k == 0:
                    act.wait_ge(in_x[h], 16)
                nc.scalar.copy(xt_h[:, h, k, :], xt[:, h, k, :]).then_inc(x_hi, 1)

            def hi_round_b(d):
                act.wait_ge(b_done, d + 1)
                nc.scalar.copy(cw_h[:, d, SM + RA:], ps[:, BANK_B[d], 0:RB]).then_inc(b_hi, 1)

            def exponential(n):
                act.wait_ge(exp_in, n + 1)
                nc.scalar.activation(expd[:], diff[:], ACT.Exp).then_inc(exp_out, 1)

            def hi_gated(n, h, layer):
                act.wait_ge(t_done, n + 1)
                nc.scalar.copy(gt_h[:, layer, h, :], ps[:, BANK_T[layer], :]).then_inc(t_hi, 1)

            for k in range(KC):
                act.wait_ge(in_s1[k], 16)
                nc.scalar.copy(s1_h[:, k, :], s1[:, k, :]).then_inc(s1_hi, 1)
            act.wait_ge(in_m2b, 16)
            nc.scalar.copy(m2b_h[:], m2b[:]).then_inc(m2b_hi, 1)
            for d in range(NS):
                act.wait_ge(a_done, d + 1)
                nc.scalar.copy(cw_h[:, d, SM:SM + RA], ps[:, d, 0:RA]).then_inc(a_hi, 1)
            act.wait_ge(in_m1, 16)
            nc.scalar.copy(cw_h[:, 0:KC, 0:SM], m1[:]).then_inc(m1_hi, 1)
            for k in range(KC):
                hi_x(0, k)
                hi_round_b(k)
            hi_round_b(KC)
            for k in range(KC):
                hi_x(1, k)
            act.wait_ge(in_b2, 16)
            nc.scalar.copy(b2_h[:], b2[:]).then_inc(b2_hi, 1)
            n = 0
            for h in range(HALVES):
                for layer in range(2):
                    exponential(n)
                    hi_gated(n, h, layer)
                    n += 1

        @block.vector
        def _(dve):
            steps = [0]

            def then(instruction):
                steps[0] += 1
                instruction.then_inc(dve_step, 1)
                dve.wait_ge(dve_step, steps[0])

            def lo(out, whole, hi):
                return nc.vector.tensor_tensor(out, whole, hi.bitcast(f32), ALU.subtract)

            def lo_x(h, k):
                if k == 0:
                    dve.wait_ge(in_x[h], 16)
                dve.wait_ge(x_hi, KC * h + k + 1)
                lo(xt_l[:, h, k, :], xt[:, h, k, :], xt_h[:, h, k, :]).then_inc(x_lo, 1)

            def lo_round_b(d):
                dve.wait_ge(b_done, d + 1)
                dve.wait_ge(b_hi, d + 1)
                lo(cw_l[:, d, SM + RA:], ps[:, BANK_B[d], 0:RB], cw_h[:, d, SM + RA:]).then_inc(b_lo, 1)

            def gates(n, h, layer):
                c = SM * layer
                if layer == 0:
                    dve.wait_ge(small1_done, TILES * (h + 1))
                    then(nc.vector.scalar_tensor_tensor(logit[:], lang[:, TILES * h:TILES * (h + 1), :], LANG_BIAS,
                                                        small[:, :, c + ER:c + SM], ALU.mult, ALU.add))
                else:
                    dve.wait_ge(small2_done, TILES * (h + 1))
                    then(nc.vector.tensor_copy(logit[:], small[:, :, c + ER:c + SM]))
                for i in range(TILES):
                    last = nc.vector.max(top[:, i, :], logit[:, i, :])
                    if i < TILES - 1:
                        last.then_inc(dve_step, 1)
                        steps[0] += 1
                then(last)
                nc.vector.tensor_tensor(diff[:], top[:, :, 1], top[:, :, 0], ALU.subtract).then_inc(exp_in, 1)
                for i in range(TILES):
                    last = nc.vector.max_index(place[:, i, :], top[:, i, :], logit[:, i, :])
                    if i < TILES - 1:
                        last.then_inc(dve_step, 1)
                        steps[0] += 1
                then(last)
                then(nc.vector.tensor_tensor(
                    hot[:], iota[:].unsqueeze(1).unsqueeze(1).to_broadcast([P, TILES, 2, E]),
                    place[:, :, 0:2].unsqueeze(3).to_broadcast([P, TILES, 2, E]), ALU.is_equal))
                dve.wait_ge(exp_out, n + 1)
                then(nc.vector.tensor_scalar(den[:], expd[:], 0.5, 0.5, ALU.mult, ALU.add))
                then(nc.vector.reciprocal(pair[:, :, 0], den[:]))
                then(nc.vector.tensor_tensor(pair[:, :, 1], pair[:, :, 0], expd[:], ALU.mult))
                then(nc.vector.tensor_tensor(hotw[:], hot[:], pair[:].unsqueeze(3).to_broadcast([P, TILES, 2, E]),
                                             ALU.mult))
                then(nc.vector.tensor_tensor(gate[:], hotw[:, :, 0, :], hotw[:, :, 1, :], ALU.add))
                if n:
                    dve.wait_ge(t_done, n)
                nc.vector.tensor_tensor(
                    gated[:].rearrange("p t (e r) -> p t e r", e=E),
                    small[:, :, c:c + ER].rearrange("p t (e r) -> p t e r", e=E),
                    gate[:].unsqueeze(3).to_broadcast([P, TILES, E, R]), ALU.mult).then_inc(gated_done, 1)

            def lo_gated(n, h, layer):
                dve.wait_ge(t_done, n + 1)
                dve.wait_ge(t_hi, n + 1)
                lo(gt_l[:, layer, h, :], ps[:, BANK_T[layer], :], gt_h[:, layer, h, :]).then_inc(t_lo, 1)

            def finish(h, j):
                dve.wait_ge(z_done, KC * h + j + 1)
                nc.vector.scalar_tensor_tensor(result[:, j, h, :], ps[:, BANK_Z[j], :], bias[:, j:j + 1],
                                               xt[:, h, j, :], ALU.add, ALU.add).then_inc(z_out, 1)

            nc.vector.memset(warm[:].bitcast(f32), 0.0).then_inc(warm_set, 1)
            for k in range(KC):
                dve.wait_ge(in_s1[k], 16)
                dve.wait_ge(s1_hi, k + 1)
                lo(s1_l[:, k, :], s1[:, k, :], s1_h[:, k, :]).then_inc(s1_lo, 1)
            dve.wait_ge(in_m2b, 16)
            dve.wait_ge(m2b_hi, 1)
            lo(m2b_l[:], m2b[:], m2b_h[:]).then_inc(m2b_lo, 1)
            for d in range(NS):
                dve.wait_ge(a_done, d + 1)
                dve.wait_ge(a_hi, d + 1)
                lo(cw_l[:, d, SM:SM + RA], ps[:, d, 0:RA], cw_h[:, d, SM:SM + RA]).then_inc(a_lo, 1)
            dve.wait_ge(in_m1, 16)
            dve.wait_ge(m1_hi, 1)
            lo(cw_l[:, 0:KC, 0:SM], m1[:], cw_h[:, 0:KC, 0:SM]).then_inc(m1_lo, 1)
            for k in range(KC):
                lo_x(0, k)
                lo_round_b(k)
            lo_round_b(KC)
            dve.wait_ge(iota_set, 1)
            then(nc.vector.tensor_copy(iota[:], iota_i[:]))
            dve.wait_ge(in_ids, 16)
            then(nc.vector.tensor_tensor(lang[:], ids[:].unsqueeze(2).to_broadcast([P, NB, E]),
                                         iota[:].unsqueeze(1).to_broadcast([P, NB, E]), ALU.is_equal))
            for k in range(KC):
                lo_x(1, k)
            dve.wait_ge(in_b2, 16)
            dve.wait_ge(b2_hi, 1)
            lo(b2_l[:], b2[:], b2_h[:]).then_inc(b2_lo, 1)
            gates(0, 0, 0)
            lo_gated(0, 0, 0)
            gates(1, 0, 1)
            lo_gated(1, 0, 1)
            dve.wait_ge(in_bias, 16)
            finish(0, 0)
            gates(2, 1, 0)
            for j in range(1, KC):
                finish(0, j)
            lo_gated(2, 1, 0)
            gates(3, 1, 1)
            lo_gated(3, 1, 1)
            for j in range(KC):
                finish(1, j)

        @block.tensor
        def _(pe):
            def product(out, lhs, rhs, start, stop, again=False):
                nc.tensor.matmul(out, lhs[0], rhs[0], start=start, stop=False, skip_group_check=again)
                nc.tensor.matmul(out, lhs[0], rhs[1], start=False, stop=False, skip_group_check=again)
                return nc.tensor.matmul(out, lhs[1], rhs[0], start=False, stop=stop, skip_group_check=again)

            def weight(k, d):
                return [t[:, k, d * P:(d + 1) * P] for t in (s1_h, s1_l)]

            def m2a(k):
                return [t[:, k, S1W:] for t in (s1_h, s1_l)]

            def small_sums(h, i):
                for k in range(KC):
                    if h == 0 and i == 0 or h == 1 and i == 1:
                        pe.wait_ge(x_lo, KC * h + k + 1)
                    last = product(ps[:, BANK_SMALL + i, 0:2 * SM],
                                   [t[:, h, k, i * P:(i + 1) * P] for t in (xt_h, xt_l)],
                                   [t[:, k, 0:2 * SM] for t in (cw_h, cw_l)], k == 0, k == KC - 1)
                last.then_inc(small1_done, 1)

            def z_part(h, j):
                for k in range(KC):
                    product(ps[:, BANK_Z[j], :],
                            [t[:, k, 2 * SM + j * P:2 * SM + (j + 1) * P] for t in (cw_h, cw_l)],
                            [t[:, h, k, :] for t in (xt_h, xt_l)], k == 0, False)

            def z_lora1(h, j):
                product(ps[:, BANK_Z[j], :],
                        [t[:, KC, 2 * SM + j * P:2 * SM + (j + 1) * P] for t in (cw_h, cw_l)],
                        [t[:, 0, h, :] for t in (gt_h, gt_l)], False, False)

            def z_lora2(h, j):
                product(ps[:, BANK_Z[j], :], [t[:, j * P:(j + 1) * P] for t in (b2_h, b2_l)],
                        [t[:, 1, h, :] for t in (gt_h, gt_l)], False, True).then_inc(z_done, 1)

            def transposes(n, layer):
                pe.wait_ge(gated_done, n + 1)
                for i in range(TILES):
                    last = nc.tensor.transpose(ps[:, BANK_T[layer], i * P:(i + 1) * P], gated[:, i, :], ident[:])
                last.then_inc(t_done, 1)

            def small_lora(n, h):
                pe.wait_ge(t_lo, n + 1)
                for i in range(TILES):
                    product(ps[:, BANK_SMALL + i, SM:2 * SM], [t[:, 0, h, i * P:(i + 1) * P] for t in (gt_h, gt_l)],
                            [t[:, KC, SM:2 * SM] for t in (cw_h, cw_l)], False, True, again=True).then_inc(small2_done, 1)

            pe.wait_ge(warm_set, 1)
            for _ in range(WARMUPS):
                nc.tensor.matmul(ps[:, BANK_B[2], :], warm[:, 0:P], warm[:], start=True, stop=True)

            for k in range(KC):
                pe.wait_ge(s1_hi, k + 1)
                if k < KC - 1:
                    for d in range(NS):
                        nc.tensor.matmul(ps[:, d, 0:RA], weight(k, d)[0], m2a(k)[0], start=k == 0, stop=False)
                    pe.wait_ge(s1_lo, k + 1)
                    for d in range(NS):
                        nc.tensor.matmul(ps[:, d, 0:RA], weight(k, d)[0], m2a(k)[1], start=False, stop=False)
                        nc.tensor.matmul(ps[:, d, 0:RA], weight(k, d)[1], m2a(k)[0], start=False, stop=False)
                else:
                    pe.wait_ge(s1_lo, k + 1)
                    for d in range(NS):
                        product(ps[:, d, 0:RA], weight(k, d), m2a(k), False, True).then_inc(a_done, 1)
            pe.wait_ge(m2b_lo, 1)
            for d in range(NS):
                if BANK_B[d] < NS:
                    pe.wait_ge(a_lo, BANK_B[d] + 1)
                for k in range(KC):
                    last = product(ps[:, BANK_B[d], 0:RB], weight(k, d), [t[:, k, :] for t in (m2b_h, m2b_l)],
                                   k == 0, k == KC - 1)
                last.then_inc(b_done, 1)

            pe.wait_ge(a_lo, NS)
            pe.wait_ge(m1_lo, 1)
            for i in range(TILES):
                if i == TILES - 1:
                    pe.wait_ge(b_lo, 1)
                small_sums(0, i)
            for h in range(HALVES):
                n = 2 * h
                if h == 0:
                    pe.wait_ge(b_lo, NS)
                for j in (0, 1):
                    if h == 1:
                        pe.wait_ge(z_out, j + 1)
                    z_part(h, j)
                if h == 0:
                    pe.wait_ge(ident_set, 2)
                else:
                    pe.wait_ge(z_out, KC)
                transposes(n, 0)
                z_part(h, 2)
                small_lora(n, h)
                z_part(h, 3)
                z_lora1(h, 0)
                z_lora1(h, 1)
                transposes(n + 1, 1)
                z_lora1(h, 2)
                z_lora1(h, 3)
                if h == 0:
                    for i in (1, 2, 3):
                        small_sums(1, i)
                    pe.wait_ge(t_lo, 2)
                    small_sums(1, 0)
                    pe.wait_ge(b2_lo, 1)
                pe.wait_ge(t_lo, n + 2)
                for j in range(KC):
                    z_lora2(h, j)


def kernel(x, itok_B_0_7, L0_cond_W, L0_cond_Wr, L0_cond_A, L0_cond_B, L0_ffn_W_base, L0_ffn_b_base, L0_ffn_W_router,
           L0_ffn_A, L0_ffn_B):
    import numpy as np
    import concourse.bacc as bacc
    from concourse.bass_utils import run_bass_kernel_spmd

    def chunks(a):
        return a.reshape(KC, P, a.shape[1]).transpose(1, 0, 2)

    f = np.asarray
    x, w1, w2 = f(x), f(L0_cond_W), f(L0_ffn_W_base)
    b1t = f(L0_cond_B).transpose(1, 0, 2).reshape(D, ER)
    a1t = f(L0_cond_A).reshape(ER, D).T
    a2t = f(L0_ffn_A).reshape(ER, D).T
    m2t = np.concatenate([a2t, f(L0_ffn_W_router).T, w2.T], axis=1)
    arrays = {
        "s1": np.concatenate([w1, b1t, m2t[:, :RA]], axis=1).reshape(KC, P, S1W + RA),
        "xt": x.reshape(HALVES, HT, KC, P).transpose(0, 3, 2, 1),
        "m1": chunks(np.concatenate([a1t, f(L0_cond_Wr).T], axis=1)),
        "m2b": chunks(m2t[:, RA:]),
        "b2": f(L0_ffn_B).transpose(0, 2, 1).reshape(ER, D),
        "bias": f(L0_ffn_b_base).reshape(KC, P).T,
        "ids": np.broadcast_to(f(itok_B_0_7), (P, NB)),
    }
    arrays = {f"in_{n}": np.ascontiguousarray(a) for n, a in arrays.items()}
    nc = bacc.Bacc("TRN2", target_bir_lowering=False, num_devices=1)
    args = [nc.dram_tensor(n, a.shape, mybir.dt.from_np(a.dtype), kind="ExternalInput").ap()
            for n, a in arrays.items()]
    out = nc.dram_tensor("out", (HALVES, KC, P, HT), mybir.dt.float32, kind="ExternalOutput").ap()
    adaln_ffn(nc, *args, out)
    r = run_bass_kernel_spmd(nc, [arrays], core_ids=[0])
    return f(r.results[0]["out"]).transpose(0, 3, 1, 2).reshape(NB, P, D)
```

```python
import concourse.bass as bass
from concourse import mybir
from contextlib import ExitStack

P = 128
D = 512
KC = D // P
E = 8
R = 16
ER = E * R
NB = 8
TOKENS = NB * P
HALVES = 2
HT = TOKENS // HALVES
TILES = HT // P
SM = ER + E
CW = 2 * SM + D
M2W = SM + D
RA = M2W // 2
RB = M2W - RA
S1W = D + ER
NS = S1W // P
S1_PIECES = [(k, a, b) for k in range(2) for a, b in ((0, RA + 2 * P), (RA + 2 * P, RA + S1W))]
S1_PIECES += [(k, 0, RA + S1W) for k in range(2, KC)]
Q = HT // 2
BANK_B = (5, 6, 7, 0, 1)
BANK_SMALL = 2
BANK_Z = (6, 7, 0, 1)
BANK_T = (BANK_Z[3], BANK_SMALL)
BANK_LAST = BANK_SMALL + 2
Z_PIECES = [(h, j, BANK_Z[j], 0, HT) for h in range(HALVES) for j in range(KC)]
Z_PIECES[-1:] = [(HALVES - 1, KC - 1, BANK_Z[KC - 1], 0, Q), (HALVES - 1, KC - 1, BANK_LAST, Q, HT)]
LANG_BIAS = 5.0
WARMUPS = 11


def adaln_ffn(nc: bass.Bass, s1_d, xt_d, m1_d, m2b_d, b2_d, bias_d, ids_d, out_d):
    f32, f32r = mybir.dt.float32, mybir.dt.float32r
    bf16 = mybir.dt.bfloat16
    i32, u32 = mybir.dt.int32, mybir.dt.uint32
    ALU = mybir.AluOpType
    ACT = mybir.ActivationFunctionType

    with ExitStack() as ctx:
        def sb(name, shape, dt):
            return ctx.enter_context(nc.sbuf_tensor(name, shape, dt))

        def sem(name):
            return ctx.enter_context(nc.semaphore(name))

        s1 = sb("s1", [P, KC, S1W + RA], f32)
        m2b = sb("m2b", [P, KC, RB], f32)
        m1 = sb("m1", [P, KC, SM], f32)
        b2 = sb("b2", [P, D], f32)
        xt = sb("xt", [P, HALVES, KC, HT], f32)
        bias = sb("bias", [P, KC], f32)
        ids = sb("ids", [P, NB], i32)
        s1_h, s1_l = sb("s1_h", [P, KC, S1W + RA], f32r), sb("s1_l", [P, KC, S1W + RA], f32r)
        m2b_h, m2b_l = sb("m2b_h", [P, KC, RB], f32r), sb("m2b_l", [P, KC, RB], f32r)
        b2_h, b2_l = sb("b2_h", [P, D], f32r), sb("b2_l", [P, D], f32r)
        xt_h, xt_l = sb("xt_h", [P, HALVES, KC, HT], f32r), sb("xt_l", [P, HALVES, KC, HT], f32r)
        cw_h, cw_l = sb("cw_h", [P, NS, CW], f32r), sb("cw_l", [P, NS, CW], f32r)
        gt_h, gt_l = sb("gt_h", [P, 2, HALVES, HT], f32r), sb("gt_l", [P, 2, HALVES, HT], f32r)
        ident = sb("ident", [P, P], f32)
        iota_i = sb("iota_i", [P, E], i32)
        iota = sb("iota", [P, E], f32)
        lang = sb("lang", [P, NB, E], f32)
        logit = sb("logit", [P, TILES, E], f32)
        top = sb("top", [P, TILES, E], f32)
        place = sb("place", [P, TILES, E], u32)
        diff = sb("diff", [P, TILES], f32)
        expd = sb("expd", [P, TILES], f32)
        den = sb("den", [P, TILES], f32)
        pair = sb("pair", [P, TILES, 2], f32)
        hot = sb("hot", [P, TILES, 2, E], f32)
        hotw = sb("hotw", [P, TILES, 2, E], f32)
        gate = sb("gate", [P, TILES, E], f32)
        gated = sb("gated", [P, TILES, ER], f32)
        result = sb("result", [P, KC, HALVES, HT], f32)

        ps = ctx.enter_context(nc.psum_tensor("ps", [P, 8, 512], f32))
        small = ps[:, BANK_SMALL:BANK_SMALL + TILES, :]

        in_s1 = [sem(f"in_s1_{n}") for n in range(len(S1_PIECES))]
        in_m2b, in_m1, in_b2 = sem("in_m2b"), sem("in_m1"), sem("in_b2")
        in_bias, in_ids = sem("in_bias"), sem("in_ids")
        in_x = [sem(f"in_x_{h}") for h in range(HALVES)]
        ident_set = sem("ident_set")
        iota_set = sem("iota_set")
        s1_hi, s1_lo = sem("s1_hi"), sem("s1_lo")
        m2b_hi, m2b_lo = sem("m2b_hi"), sem("m2b_lo")
        m1_hi, m1_lo = sem("m1_hi"), sem("m1_lo")
        b2_hi, b2_lo = sem("b2_hi"), sem("b2_lo")
        x_hi, x_lo = sem("x_hi"), sem("x_lo")
        a_done, b_done = sem("a_done"), sem("b_done")
        a_hi, a_lo = sem("a_hi"), sem("a_lo")
        b_hi, b_lo = sem("b_hi"), sem("b_lo")
        small1_done = sem("small1_done")
        small2_done = sem("small2_done")
        exp_in, exp_out = sem("exp_in"), sem("exp_out")
        gated_done = sem("gated_done")
        t_done = sem("t_done")
        t_hi, t_lo = sem("t_hi"), sem("t_lo")
        z_done = sem("z_done")
        z_biased = sem("z_biased")
        z_out = sem("z_out")
        stored = sem("stored")
        dve_step = sem("dve_step")

        block = ctx.enter_context(nc.Block())

        @block.sync
        def _(sp):
            for n, (k, a, b) in enumerate(S1_PIECES):
                sp.dma_start(s1[:, k, a:b], s1_d[k, :, a:b]).then_inc(in_s1[n], 16)
            sp.dma_start(m2b[:], m2b_d).then_inc(in_m2b, 16)
            sp.dma_start(m1[:], m1_d).then_inc(in_m1, 16)
            for h in range(HALVES):
                sp.dma_start(xt[:, h], xt_d[h]).then_inc(in_x[h], 16)
                if h == 0:
                    sp.dma_start(ids[:], ids_d).then_inc(in_ids, 16)
            sp.dma_start(b2[:], b2_d).then_inc(in_b2, 16)
            sp.dma_start(bias[:], bias_d).then_inc(in_bias, 16)
            for n, (h, j, _, a, b) in enumerate(Z_PIECES):
                sp.wait_ge(z_out, n + 1)
                sp.dma_start(out_d[h, j, :, a:b], result[:, j, h, a:b]).then_inc(stored, 16)
            sp.wait_ge(stored, 16 * len(Z_PIECES))

        @block.gpsimd
        def _(pool):
            nc.gpsimd.memset(ident[:], 0.0).then_inc(ident_set, 1)
            nc.gpsimd.iota(iota_i[:], [[1, E]], base=0, channel_multiplier=0).then_inc(iota_set, 1)
            pool.wait_ge(ident_set, 1)
            nc.gpsimd.affine_select(out=ident[:], in_=ident[:], compare_op=ALU.not_equal, fill=1.0, base=0,
                                    pattern=[[-1, P]], channel_multiplier=1).then_inc(ident_set, 1)

        @block.scalar
        def _(act):
            def hi_x(h, k):
                if k == 0:
                    act.wait_ge(in_x[h], 16)
                nc.scalar.copy(xt_h[:, h, k, :], xt[:, h, k, :]).then_inc(x_hi, 1)

            def hi_round_b(d):
                act.wait_ge(b_done, d + 1)
                nc.scalar.copy(cw_h[:, d, SM + RA:], ps[:, BANK_B[d], 0:RB]).then_inc(b_hi, 1)

            def exponential(n):
                act.wait_ge(exp_in, n + 1)
                nc.scalar.activation(expd[:], diff[:], ACT.Exp).then_inc(exp_out, 1)

            def take_out(n):
                h, j, bank, a, b = Z_PIECES[n]
                act.wait_ge(z_done, n + 1)
                nc.scalar.activation(result[:, j, h, a:b], ps[:, bank, a:b], ACT.Identity,
                                     bias=bias[:, j:j + 1]).then_inc(z_biased, 1)

            def hi_gated(n, h, layer):
                act.wait_ge(t_done, n + 1)
                nc.scalar.copy(gt_h[:, layer, h, :], ps[:, BANK_T[layer], :]).then_inc(t_hi, 1)

            for n, (k, a, b) in enumerate(S1_PIECES):
                act.wait_ge(in_s1[n], 16)
                nc.scalar.copy(s1_h[:, k, a:b], s1[:, k, a:b]).then_inc(s1_hi, 1)
            act.wait_ge(in_m2b, 16)
            for k in range(0, KC, 2):
                nc.scalar.copy(m2b_h[:, k:k + 2, :], m2b[:, k:k + 2, :]).then_inc(m2b_hi, 1)
            for d in range(NS):
                act.wait_ge(a_done, d + 1)
                nc.scalar.copy(cw_h[:, d, SM:SM + RA], ps[:, d, 0:RA]).then_inc(a_hi, 1)
            act.wait_ge(in_m1, 16)
            nc.scalar.copy(cw_h[:, 0:KC, 0:SM], m1[:]).then_inc(m1_hi, 1)
            for k in range(KC):
                hi_x(0, k)
                hi_round_b(k)
            hi_round_b(KC)
            for k in range(KC):
                hi_x(1, k)
            act.wait_ge(in_b2, 16)
            nc.scalar.copy(b2_h[:], b2[:]).then_inc(b2_hi, 1)
            exponential(0)
            hi_gated(0, 0, 0)
            exponential(1)
            hi_gated(1, 0, 1)
            act.wait_ge(in_bias, 16)
            take_out(0)
            exponential(2)
            take_out(1)
            take_out(2)
            take_out(3)
            hi_gated(2, 1, 0)
            exponential(3)
            hi_gated(3, 1, 1)

        @block.vector
        def _(dve):
            steps = [0]

            def then(instruction):
                steps[0] += 1
                instruction.then_inc(dve_step, 1)
                dve.wait_ge(dve_step, steps[0])

            def lo(out, whole, hi):
                return nc.vector.tensor_tensor(out, whole, hi.bitcast(f32), ALU.subtract)

            def lo_x(h, k):
                if k == 0:
                    dve.wait_ge(in_x[h], 16)
                dve.wait_ge(x_hi, KC * h + k + 1)
                lo(xt_l[:, h, k, :], xt[:, h, k, :], xt_h[:, h, k, :]).then_inc(x_lo, 1)

            def lo_round_b(d):
                dve.wait_ge(b_done, d + 1)
                dve.wait_ge(b_hi, d + 1)
                lo(cw_l[:, d, SM + RA:], ps[:, BANK_B[d], 0:RB], cw_h[:, d, SM + RA:]).then_inc(b_lo, 1)

            def gates(n, h, layer):
                c = SM * layer
                if layer == 0:
                    dve.wait_ge(small1_done, TILES * (h + 1))
                    then(nc.vector.scalar_tensor_tensor(logit[:], lang[:, TILES * h:TILES * (h + 1), :], LANG_BIAS,
                                                        small[:, :, c + ER:c + SM], ALU.mult, ALU.add))
                else:
                    dve.wait_ge(small2_done, TILES * (h + 1))
                    then(nc.vector.tensor_copy(logit[:], small[:, :, c + ER:c + SM]))
                for i in range(TILES):
                    last = nc.vector.max(top[:, i, :], logit[:, i, :])
                then(last)
                nc.vector.tensor_tensor(diff[:], top[:, :, 1], top[:, :, 0], ALU.subtract).then_inc(exp_in, 1)
                for i in range(TILES):
                    last = nc.vector.max_index(place[:, i, :], top[:, i, :], logit[:, i, :])
                then(last)
                then(nc.vector.tensor_tensor(
                    hot[:], iota[:].unsqueeze(1).unsqueeze(1).to_broadcast([P, TILES, 2, E]),
                    place[:, :, 0:2].unsqueeze(3).to_broadcast([P, TILES, 2, E]), ALU.is_equal))
                dve.wait_ge(exp_out, n + 1)
                then(nc.vector.tensor_scalar(den[:], expd[:], 0.5, 0.5, ALU.mult, ALU.add))
                then(nc.vector.reciprocal(pair[:, :, 0], den[:]))
                then(nc.vector.tensor_tensor(pair[:, :, 1], pair[:, :, 0], expd[:], ALU.mult))
                then(nc.vector.tensor_tensor(hotw[:], hot[:], pair[:].unsqueeze(3).to_broadcast([P, TILES, 2, E]),
                                             ALU.mult))
                then(nc.vector.tensor_tensor(gate[:], hotw[:, :, 0, :], hotw[:, :, 1, :], ALU.add))
                if n:
                    dve.wait_ge(t_done, n)
                nc.vector.tensor_tensor(
                    gated[:].rearrange("p t (e r) -> p t e r", e=E),
                    small[:, :, c:c + ER].rearrange("p t (e r) -> p t e r", e=E),
                    gate[:].unsqueeze(3).to_broadcast([P, TILES, E, R]), ALU.mult).then_inc(gated_done, 1)

            def lo_gated(n, h, layer):
                dve.wait_ge(t_done, n + 1)
                dve.wait_ge(t_hi, n + 1)
                lo(gt_l[:, layer, h, :], ps[:, BANK_T[layer], :], gt_h[:, layer, h, :]).then_inc(t_lo, 1)

            def add_x(n):
                h, j, _, a, b = Z_PIECES[n]
                dve.wait_ge(z_biased, n + 1)
                nc.vector.tensor_tensor(result[:, j, h, a:b], result[:, j, h, a:b], xt[:, h, j, a:b],
                                        ALU.add).then_inc(z_out, 1)

            def finish(n):
                h, j, bank, a, b = Z_PIECES[n]
                dve.wait_ge(z_done, n + 1)
                nc.vector.scalar_tensor_tensor(result[:, j, h, a:b], ps[:, bank, a:b], bias[:, j:j + 1],
                                               xt[:, h, j, a:b], ALU.add, ALU.add).then_inc(z_out, 1)

            for n, (k, a, b) in enumerate(S1_PIECES):
                dve.wait_ge(in_s1[n], 16)
                dve.wait_ge(s1_hi, n + 1)
                lo(s1_l[:, k, a:b], s1[:, k, a:b], s1_h[:, k, a:b]).then_inc(s1_lo, 1)
            dve.wait_ge(in_m2b, 16)
            for k in range(0, KC, 2):
                dve.wait_ge(m2b_hi, k // 2 + 1)
                lo(m2b_l[:, k:k + 2, :], m2b[:, k:k + 2, :], m2b_h[:, k:k + 2, :]).then_inc(m2b_lo, 1)
            for d in range(NS):
                dve.wait_ge(a_done, d + 1)
                dve.wait_ge(a_hi, d + 1)
                lo(cw_l[:, d, SM:SM + RA], ps[:, d, 0:RA], cw_h[:, d, SM:SM + RA]).then_inc(a_lo, 1)
            dve.wait_ge(in_m1, 16)
            dve.wait_ge(m1_hi, 1)
            lo(cw_l[:, 0:KC, 0:SM], m1[:], cw_h[:, 0:KC, 0:SM]).then_inc(m1_lo, 1)
            for k in range(KC):
                lo_x(0, k)
                lo_round_b(k)
            lo_round_b(KC)
            dve.wait_ge(iota_set, 1)
            then(nc.vector.tensor_copy(iota[:], iota_i[:]))
            dve.wait_ge(in_ids, 16)
            then(nc.vector.tensor_tensor(lang[:], ids[:].unsqueeze(2).to_broadcast([P, NB, E]),
                                         iota[:].unsqueeze(1).to_broadcast([P, NB, E]), ALU.is_equal))
            for k in range(KC):
                lo_x(1, k)
            dve.wait_ge(in_b2, 16)
            dve.wait_ge(b2_hi, 1)
            lo(b2_l[:], b2[:], b2_h[:]).then_inc(b2_lo, 1)
            gates(0, 0, 0)
            lo_gated(0, 0, 0)
            gates(1, 0, 1)
            lo_gated(1, 0, 1)
            gates(2, 1, 0)
            lo_gated(2, 1, 0)
            for n in range(KC - 1):
                add_x(n)
            gates(3, 1, 1)
            add_x(KC - 1)
            lo_gated(3, 1, 1)
            dve.wait_ge(in_bias, 16)
            for n in range(KC, len(Z_PIECES)):
                finish(n)

        @block.tensor
        def _(pe):
            def product(out, lhs, rhs, start, stop, again=False):
                nc.tensor.matmul(out, lhs[0], rhs[0], start=start, stop=False, skip_group_check=again)
                nc.tensor.matmul(out, lhs[0], rhs[1], start=False, stop=False, skip_group_check=again)
                return nc.tensor.matmul(out, lhs[1], rhs[0], start=False, stop=stop, skip_group_check=again)

            def weight(k, d):
                return [t[:, k, RA + d * P:RA + (d + 1) * P] for t in (s1_h, s1_l)]

            def m2a(k):
                return [t[:, k, 0:RA] for t in (s1_h, s1_l)]

            def small_sums(h, i):
                for k in range(KC):
                    if h == 0 and i == 0 or h == 1 and i == 1:
                        pe.wait_ge(x_lo, KC * h + k + 1)
                    last = product(ps[:, BANK_SMALL + i, 0:2 * SM],
                                   [t[:, h, k, i * P:(i + 1) * P] for t in (xt_h, xt_l)],
                                   [t[:, k, 0:2 * SM] for t in (cw_h, cw_l)], k == 0, k == KC - 1)
                last.then_inc(small1_done, 1)

            def z_part(n, chunks=range(KC)):
                h, j, bank, a, b = Z_PIECES[n]
                for k in chunks:
                    product(ps[:, bank, a:b],
                            [t[:, k, 2 * SM + j * P:2 * SM + (j + 1) * P] for t in (cw_h, cw_l)],
                            [t[:, h, k, a:b] for t in (xt_h, xt_l)], k == 0, False)

            def z_lora1(n):
                h, j, bank, a, b = Z_PIECES[n]
                product(ps[:, bank, a:b], [t[:, KC, 2 * SM + j * P:2 * SM + (j + 1) * P] for t in (cw_h, cw_l)],
                        [t[:, 0, h, a:b] for t in (gt_h, gt_l)], False, False)

            def z_lora2(n):
                h, j, bank, a, b = Z_PIECES[n]
                product(ps[:, bank, a:b], [t[:, j * P:(j + 1) * P] for t in (b2_h, b2_l)],
                        [t[:, 1, h, a:b] for t in (gt_h, gt_l)], False, True).then_inc(z_done, 1)

            def transposes(n, layer):
                pe.wait_ge(gated_done, n + 1)
                for i in range(TILES):
                    last = nc.tensor.transpose(ps[:, BANK_T[layer], i * P:(i + 1) * P], gated[:, i, :], ident[:])
                last.then_inc(t_done, 1)

            def small_lora(n, h):
                pe.wait_ge(t_lo, n + 1)
                for i in range(TILES):
                    product(ps[:, BANK_SMALL + i, SM:2 * SM], [t[:, 0, h, i * P:(i + 1) * P] for t in (gt_h, gt_l)],
                            [t[:, KC, SM:2 * SM] for t in (cw_h, cw_l)], False, True, again=True).then_inc(small2_done, 1)

            ones = [nc.const_aps.tensor(1.0, [P, n], bf16) for n in (P, 512)]
            for _ in range(WARMUPS):
                nc.tensor.matmul(ps[:, BANK_B[2], :], ones[0], ones[1], start=True, stop=True)

            def pieces_to(k, d):
                return 1 + max(n for n, (kk, a, _) in enumerate(S1_PIECES) if kk == k and a < RA + (d + 1) * P)

            for k in range(KC - 1):
                for d in range(NS):
                    pe.wait_ge(s1_hi, pieces_to(k, d))
                    nc.tensor.matmul(ps[:, d, 0:RA], weight(k, d)[0], m2a(k)[0], start=k == 0, stop=False)
                for d in range(NS):
                    pe.wait_ge(s1_lo, pieces_to(k, d))
                    nc.tensor.matmul(ps[:, d, 0:RA], weight(k, d)[0], m2a(k)[1], start=False, stop=False)
                    nc.tensor.matmul(ps[:, d, 0:RA], weight(k, d)[1], m2a(k)[0], start=False, stop=False)
            pe.wait_ge(s1_lo, len(S1_PIECES))
            for d in range(NS):
                product(ps[:, d, 0:RA], weight(KC - 1, d), m2a(KC - 1), False, True).then_inc(a_done, 1)
            for d in range(NS):
                if BANK_B[d] < NS:
                    pe.wait_ge(a_lo, BANK_B[d] + 1)
                for k in range(KC):
                    if d == 0 and k % 2 == 0:
                        pe.wait_ge(m2b_lo, k // 2 + 1)
                    last = product(ps[:, BANK_B[d], 0:RB], weight(k, d), [t[:, k, :] for t in (m2b_h, m2b_l)],
                                   k == 0, k == KC - 1)
                last.then_inc(b_done, 1)

            pe.wait_ge(a_lo, NS)
            pe.wait_ge(m1_lo, 1)
            for i in range(TILES):
                if i == TILES - 1:
                    pe.wait_ge(b_lo, 1)
                small_sums(0, i)
            pe.wait_ge(b_lo, NS)
            z_part(0)
            z_part(1)
            pe.wait_ge(ident_set, 2)
            transposes(0, 0)
            z_part(2)
            small_lora(0, 0)
            z_part(3)
            for n in range(KC):
                z_lora1(n)
            transposes(1, 1)
            for i in (1, 2, 3):
                small_sums(1, i)
            pe.wait_ge(t_lo, 2)
            small_sums(1, 0)
            pe.wait_ge(b2_lo, 1)
            for n in range(KC):
                z_lora2(n)
            pe.wait_ge(z_biased, 1)
            z_part(4, [0, 1])
            pe.wait_ge(z_biased, KC)
            transposes(2, 0)
            z_part(4, [2, 3])
            z_part(5, [0])
            small_lora(2, 1)
            z_part(5, [1, 2, 3])
            z_part(6, [0])
            z_lora1(4)
            z_lora1(5)
            transposes(3, 1)
            z_part(6, [1, 2, 3])
            pe.wait_ge(t_lo, 4)
            z_lora2(4)
            z_lora2(5)
            z_lora1(6)
            z_lora2(6)
            for n in range(7, len(Z_PIECES)):
                z_part(n)
                z_lora1(n)
                z_lora2(n)


def kernel(x, itok_B_0_7, L0_cond_W, L0_cond_Wr, L0_cond_A, L0_cond_B, L0_ffn_W_base, L0_ffn_b_base, L0_ffn_W_router,
           L0_ffn_A, L0_ffn_B):
    import numpy as np
    import concourse.bacc as bacc
    from concourse.bass_utils import run_bass_kernel_spmd

    def chunks(a):
        return a.reshape(KC, P, a.shape[1]).transpose(1, 0, 2)

    f = np.asarray
    x, w1, w2 = f(x), f(L0_cond_W), f(L0_ffn_W_base)
    b1t = f(L0_cond_B).transpose(1, 0, 2).reshape(D, ER)
    a1t = f(L0_cond_A).reshape(ER, D).T
    a2t = f(L0_ffn_A).reshape(ER, D).T
    m2t = np.concatenate([a2t, f(L0_ffn_W_router).T, w2.T], axis=1)
    arrays = {
        "s1": np.concatenate([m2t[:, :RA], w1, b1t], axis=1).reshape(KC, P, S1W + RA),
        "xt": x.reshape(HALVES, HT, KC, P).transpose(0, 3, 2, 1),
        "m1": chunks(np.concatenate([a1t, f(L0_cond_Wr).T], axis=1)),
        "m2b": chunks(m2t[:, RA:]),
        "b2": f(L0_ffn_B).transpose(0, 2, 1).reshape(ER, D),
        "bias": f(L0_ffn_b_base).reshape(KC, P).T,
        "ids": np.broadcast_to(f(itok_B_0_7), (P, NB)),
    }
    arrays = {f"in_{n}": np.ascontiguousarray(a) for n, a in arrays.items()}
    nc = bacc.Bacc("TRN2", target_bir_lowering=False, num_devices=1)
    args = [nc.dram_tensor(n, a.shape, mybir.dt.from_np(a.dtype), kind="ExternalInput").ap()
            for n, a in arrays.items()]
    out = nc.dram_tensor("out", (HALVES, KC, P, HT), mybir.dt.float32, kind="ExternalOutput").ap()
    adaln_ffn(nc, *args, out)
    r = run_bass_kernel_spmd(nc, [arrays], core_ids=[0])
    return f(r.results[0]["out"]).transpose(0, 3, 1, 2).reshape(NB, P, D)
```
